# Optimizing a Trainium2 kernel written in Bass

```python
import numpy as np
import jax
import jax.numpy as jnp

def _softmax(x, axis=-1):
    return jax.nn.softmax(x, axis=axis)

def _gelu(x):
    return jax.nn.gelu(x, approximate=True)

def _silu(x):
    return jax.nn.silu(x)

def _sigmoid(x):
    return jax.nn.sigmoid(x)

def _layernorm(x, axis=-1, eps=1e-05):
    m = jnp.mean(x, axis=axis, keepdims=True)
    v = jnp.var(x, axis=axis, keepdims=True)
    return (x - m) / jnp.sqrt(v + eps)

def _scatter_add(tgt, idx, src, axis=0):
    return tgt.at[idx].add(src)

def _segment_sum(src, seg, n):
    return jax.ops.segment_sum(src, seg, n)
kernel_name = 'mk_cond_resid_d2_seqx_r4_6747dd'

def setup_inputs(seed: int=0):
    np.random.seed(seed)
    _w = jnp.asarray

    def _rec_inputs():
        import jax
        import jax.numpy as jnp
        _rk = jax.random.key(seed)
        x = -0.000125 + 0.9999 * jax.random.normal(jax.random.fold_in(_rk, 1), (8, 256, 1024), jnp.float32)
        _lenS = 256 - jax.random.randint(jax.random.fold_in(_rk, 7), (8,), 0, max(1, 256 // 4) + 1, jnp.int32)
        _lenS2 = 256 - jax.random.randint(jax.random.fold_in(_rk, 8), (8,), 0, max(1, 256 // 4) + 1, jnp.int32)
        itok_B_0_23 = jax.random.randint(jax.random.fold_in(_rk, 11), (8,), 0, 24, jnp.int32)
        itok_B_6_15 = jax.random.randint(jax.random.fold_in(_rk, 12), (8,), 6, 16, jnp.int32)
        return (x, itok_B_0_23, itok_B_6_15)
    x, itok_B_0_23, itok_B_6_15 = _rec_inputs()

    def _L0_cond_setup():
        import jax, jax.numpy as jnp
        import numpy as np
        R = 16
        ALPHA = 32
        SCALING = ALPHA / R
        SLOTS = 32
        IN_F = 1024
        OUT_F = 1024
        B, T = (8, 256)
        key = jax.random.key(seed)
        k1, k2, k3, k4, k5, k6 = jax.random.split(key, 6)
        x = jax.random.normal(k1, (B, T, IN_F), dtype=jnp.float32)
        adapter_mapping = jax.random.randint(k2, (B,), 0, SLOTS, dtype=jnp.int32)
        W = jax.random.normal(k3, (OUT_F, IN_F), dtype=jnp.float32) * 0.02
        b = jax.random.normal(k4, (OUT_F,), dtype=jnp.float32) * 0.02
        lora_As = jax.random.normal(k5, (SLOTS, IN_F, R), dtype=jnp.float32) * 0.02
        lora_Bs = jax.random.normal(k6, (SLOTS, R, OUT_F), dtype=jnp.float32) * 0.02
        return {'x': x, 'adapter_mapping': adapter_mapping, 'W': W, 'b': b, 'lora_As': lora_As, 'lora_Bs': lora_Bs}
    _L0_cond_all = _L0_cond_setup()
    _L0_cond_in = {k: v for k, v in _L0_cond_all.items() if k in ('W', 'b', 'lora_As', 'lora_Bs')}
    del _L0_cond_all

    def _L1_cond_setup():
        import jax, jax.numpy as jnp
        import numpy as np
        B, S, D_IN, D_OUT = (4, 512, 1024, 1024)
        RANK, MAX_LORAS = (16, 32)
        key = jax.random.key(seed)
        ks = jax.random.split(key, 6)
        x = jax.random.normal(ks[0], (B, S, D_IN), dtype=jnp.float32)
        adapter_ids = jax.random.randint(ks[1], (B,), 0, MAX_LORAS)
        base_weight = jax.random.normal(ks[2], (D_OUT, D_IN), dtype=jnp.float32) * D_IN ** (-0.5)
        base_bias = jax.random.normal(ks[3], (D_OUT,), dtype=jnp.float32) * 0.01
        lora_A_w = jax.random.normal(ks[4], (MAX_LORAS, RANK, D_IN), dtype=jnp.float32) * D_IN ** (-0.5)
        lora_B_w = jax.random.normal(ks[5], (MAX_LORAS, D_OUT, RANK), dtype=jnp.float32) * RANK ** (-0.5)
        return {'x': x, 'adapter_ids': adapter_ids, 'base_weight': base_weight, 'base_bias': base_bias, 'lora_A_w': lora_A_w, 'lora_B_w': lora_B_w}
    _L1_cond_all = _L1_cond_setup()
    _L1_cond_in = {k: v for k, v in _L1_cond_all.items() if k in ('base_weight', 'base_bias', 'lora_A_w', 'lora_B_w')}
    del _L1_cond_all
    return {'x': x, 'itok_B_0_23': itok_B_0_23, 'itok_B_6_15': itok_B_6_15, 'L0_cond_W': _L0_cond_in['W'], 'L0_cond_b': _L0_cond_in['b'], 'L0_cond_lora_As': _L0_cond_in['lora_As'], 'L0_cond_lora_Bs': _L0_cond_in['lora_Bs'], 'L1_cond_base_weight': _L1_cond_in['base_weight'], 'L1_cond_base_bias': _L1_cond_in['base_bias'], 'L1_cond_lora_A_w': _L1_cond_in['lora_A_w'], 'L1_cond_lora_B_w': _L1_cond_in['lora_B_w']}

def reference(x, itok_B_0_23, itok_B_6_15, L0_cond_W, L0_cond_b, L0_cond_lora_As, L0_cond_lora_Bs, L1_cond_base_weight, L1_cond_base_bias, L1_cond_lora_A_w, L1_cond_lora_B_w):
    import jax
    import jax.numpy as jnp

    def _L0_cond_ref(x, adapter_mapping, W, b, lora_As, lora_Bs):
        import jax, jax.numpy as jnp
        import numpy as np
        R = 16
        ALPHA = 32
        SCALING = ALPHA / R
        SLOTS = 32
        IN_F = 1024
        OUT_F = 1024
        B, T = (8, 256)
        base_out = jnp.einsum('bti,oi->bto', x, W) + b
        A = lora_As[adapter_mapping]
        Bm = lora_Bs[adapter_mapping]
        lora_h = jnp.einsum('bti,bir->btr', x, A)
        lora_out = jnp.einsum('btr,bro->bto', lora_h, Bm)
        return base_out + lora_out * SCALING

    def _L1_cond_ref(x, adapter_ids, base_weight, base_bias, lora_A_w, lora_B_w):
        import jax, jax.numpy as jnp
        import numpy as np
        B, S, D_IN, D_OUT = (4, 512, 1024, 1024)
        RANK, MAX_LORAS = (16, 32)
        result = jnp.einsum('bsd,od->bso', x, base_weight) + base_bias
        A = lora_A_w[adapter_ids]
        Bw = lora_B_w[adapter_ids]
        h = jnp.einsum('bsd,brd->bsr', x, A)
        lora_out = jnp.einsum('bsr,bor->bso', h, Bw)
        result = result + lora_out
        return result.astype(x.dtype)
    x = x + _L0_cond_ref(x, itok_B_0_23, L0_cond_W, L0_cond_b, L0_cond_lora_As, L0_cond_lora_Bs)
    x = x + _L1_cond_ref(x, itok_B_6_15, L1_cond_base_weight, L1_cond_base_bias, L1_cond_lora_A_w, L1_cond_lora_B_w)
    return x

_drawn_inputs = setup_inputs


def setup_inputs(seed=0):
    import zlib

    import numpy as np

    out = dict(_drawn_inputs(seed))
    spreads = {}
    factors = {'L0_cond_b': 4.125, 'L1_cond_base_bias': 8.0}
    for name, (base, spread) in spreads.items():
        noise = np.random.default_rng([zlib.crc32(name.encode()), seed]).standard_normal(out[name].shape)
        drawn = base * np.exp(spread * noise) if base else spread * noise
        out[name] = jnp.asarray(drawn.astype(out[name].dtype))
    for name, factor in factors.items():
        out[name] = (out[name] * factor).astype(out[name].dtype)
    return out
```

```python
from contextlib import ExitStack

import concourse.bass as bass
from concourse import mybir

F32 = mybir.dt.float32
F32R = mybir.dt.float32r
I32 = mybir.dt.int32
ALU = mybir.AluOpType
ACT = mybir.ActivationFunctionType

P = 128
HALF = 512
STAGE_SLOTS = 3
BANKS_D = 6
FIRST_M = 3
DMA = 16


def lora_pair(nc, xT, W0, W1T, A0, B0T, A1T, B1, b0, b1, idx0, idx1, out):
    B, _, KT, T = xT.shape
    D = KT * P
    NH = D // HALF
    RK = A0.shape[-1]
    SLOTS = A0.shape[0]
    BR = B * RK
    assert BR == P and NH == 2 and T == 2 * P and B % 2 == 0
    QT = T // P
    STACK = 6 * RK + 2
    AUX_ST = FIRST_M

    with ExitStack() as ctx:
        def sb(name, shape, dt):
            return ctx.enter_context(nc.sbuf_tensor(name, shape, dt))

        def sem(name):
            return ctx.enter_context(nc.semaphore(name))

        w0_hi = sb("w0_hi", [P, KT, D], F32R)
        w0_lo = sb("w0_lo", [P, KT, D], F32R)
        w1 = sb("w1", [P, 2 * KT * D], F32R)
        w1_hi = w1[:, 0:KT * D].rearrange("p (k n) -> p k n", k=KT)
        w1_lo = w1[:, KT * D:2 * KT * D].rearrange("p (k n) -> p k n", k=KT)
        stage = sb("stage", [P, STAGE_SLOTS, 2 * D], F32)
        a1 = sb("a1", [P, KT, 2 * BR], F32R)
        b0w = sb("b0w", [P, KT, 2 * BR + 2], F32R)
        g_all = sb("g_all", [P, KT, BR], F32)
        AA_W = KT * 4 * RK + 4 * RK
        aa = sb("aa", [P, 2, AA_W], F32R)
        a0_raw = sb("a0_raw", [P, 2, KT * RK], F32)
        x_first = sb("x_first", [P, 2, KT * T], F32R)
        rows = sb("rows", [P, 4, HALF], F32)
        bias_sum = rows[:, 0:2, :].rearrange("p a n -> p (a n)")
        b1_raw = rows[:, 2:4, :].rearrange("p a n -> p (a n)")
        scratch = sb("scratch", [P, 2 * BR + 2], F32)
        s_t = sb("s_t", [P, BR], F32)
        h_sum = sb("h_sum", [2 * RK, T], F32)
        t_blk = sb("t_blk", [P, B], F32)
        ident = sb("ident", [P, P], F32)
        same_batch = sb("same_batch", [P, B, RK], F32)
        ones_b = sb("ones_b", [P, B], F32)
        b0_raw = sb("b0_raw", [P, KT], F32)
        t_sum = sb("t_sum", [P, 1], F32)
        idx = sb("idx", [1, 2 * B], I32)

        rb = w1[0:STACK, 0:B * D].rearrange("p (b n) -> p b n", b=B)
        at = B * D
        x_second = w1[:, at:at + 2 * KT * T].rearrange("p (s n) -> p s n", s=2)
        at += 2 * KT * T
        h_stack = [w1[:, at + s * T:at + (s + 1) * T] for s in range(2)]
        at += 2 * T
        c_hl = w1[0:B, at:at + 2 * D].rearrange("p (s n) -> p s n", s=2)
        at += 2 * D
        assert at <= 2 * KT * D
        x_hi = [v[:, 0, :].rearrange("p (k t) -> p k t", k=KT) for v in (x_first, x_second)]
        x_lo = [v[:, 1, :].rearrange("p (k t) -> p k t", k=KT) for v in (x_first, x_second)]
        r_hl = a1[:, :, :].rearrange("p k n -> p (k n)").rearrange("p (s n) -> p s n", s=2)
        b1_hl = b0w[:, :, :].rearrange("p k n -> p (k n)")[:, 0:2 * D].rearrange("p (s n) -> p s n", s=2)

        banks = [ctx.enter_context(nc.psum_tensor(f"bank{i}", [P, HALF], F32)) for i in range(8)]
        h_tmp = scratch[0:32, 0:T]

        w0_landed = [sem(f"w0_landed{s}") for s in range(STAGE_SLOTS)]
        w1_landed = [sem(f"w1_landed{s}") for s in range(STAGE_SLOTS)]
        lora_landed = sem("lora_landed")
        b1_landed = sem("b1_landed")
        idx_landed = sem("idx_landed")
        b0_landed = sem("b0_landed")
        bias1_landed = sem("bias1_landed")
        x_landed = [sem(f"x_landed{s}") for s in range(2)]
        a0_landed = [sem(f"a0_landed{s}") for s in range(2)]
        rb_landed = sem("rb_landed")
        stored = [sem(f"stored{s}") for s in range(4)]
        ident_made = sem("ident_made")
        masks_made = sem("masks_made")
        bias_zeroed = sem("bias_zeroed")
        diag_added = sem("diag_added")
        hi_made = sem("hi_made")
        lo_made = sem("lo_made")
        lora_hi = sem("lora_hi")
        lora_lo = sem("lora_lo")
        d_summed = sem("d_summed")
        d_hi = sem("d_hi")
        d_lo = sem("d_lo")
        aux_summed = sem("aux_summed")
        aux_copied = sem("aux_copied")
        aux_done = sem("aux_done")
        bias_step = sem("bias_step")
        st_step = sem("st_step")
        r_summed = sem("r_summed")
        c_summed = sem("c_summed")
        rc_hi = sem("rc_hi")
        b1_hi_made = sem("b1_hi_made")
        rc_lo = sem("rc_lo")
        ones_set = sem("ones_set")
        pad_set = sem("pad_set")
        aa_hi = sem("aa_hi")
        aa_ready = sem("aa_ready")
        x_hi_made = sem("x_hi_made")
        x_ready = sem("x_ready")
        h_summed = sem("h_summed")
        h_moved = sem("h_moved")
        h_added = sem("h_added")
        h_hi = sem("h_hi")
        h_ready = sem("h_ready")
        out_summed = sem("out_summed")
        out_copied = sem("out_copied")

        block = ctx.enter_context(nc.Block())

        items = [("w", k) for k in range(6)] + [("lora", 0)] + [("w", k) for k in range(6, KT)]
        LORA_ITEM = 6
        weights_to = [sum(kind == "w" for kind, _ in items[:i + 1]) for i in range(len(items))]
        slot_uses = [sum(kind == "w" and j % STAGE_SLOTS == i % STAGE_SLOTS
                         for j, (kind, _) in enumerate(items[:i + 1])) for i in range(len(items))]

        def stage_w(i, which):
            return stage[:, i % STAGE_SLOTS, which * D:(which + 1) * D]

        def stage_lora(which):
            return stage_w(LORA_ITEM, which).rearrange("p (k n) -> p k n", k=KT)

        def stage_consumed(eng, i):
            if items[i][0] == "w":
                eng.wait_ge(lo_made, 2 * weights_to[i])
            else:
                eng.wait_ge(lora_lo, 3)

        @block.sync
        def _(sp):
            def load_w(i, k):
                s = i % STAGE_SLOTS
                if i >= STAGE_SLOTS:
                    stage_consumed(sp, i - STAGE_SLOTS)
                sp.dma_start(stage_w(i, 0), W0[k * P:(k + 1) * P, :]).then_inc(w0_landed[s], DMA)
                sp.dma_start(stage_w(i, 1), W1T[k * P:(k + 1) * P, :]).then_inc(w1_landed[s], DMA)

            def load_x(s, b):
                sp.dma_start(stage[:, s, :], xT[bass.ds(b, 1), :, :, :].rearrange("b p k t -> p (b k t)")
                             ).then_inc(x_landed[s], DMA)

            def load_a0(s, b, free=None):
                slot = sp.value_load(idx[0:1, bass.ds(b, 1)], min_val=0, max_val=SLOTS - 1)
                if free is not None:
                    sp.wait_ge(aa_ready, free)
                sp.dma_start(a0_raw[:, s, :], A0[bass.ds(slot, 1), :, :, :].rearrange("s p k r -> p (s k r)")
                             ).then_inc(a0_landed[s], DMA)

            for i in range(LORA_ITEM):
                load_w(i, items[i][1])
                if i == 0:
                    sp.dma_start(idx[0:1, 0:B], idx0).then_inc(idx_landed, DMA)
                    sp.dma_start(idx[0:1, B:2 * B], idx1).then_inc(idx_landed, DMA)
                    sp.dma_start(b0_raw[:, :], b0).then_inc(b0_landed, DMA)
            sp.wait_ge(idx_landed, 2 * DMA)
            stage_consumed(sp, LORA_ITEM - STAGE_SLOTS)
            with sp.Fori(0, B) as b:
                i0 = sp.value_load(idx[0:1, bass.ds(b, 1)], min_val=0, max_val=SLOTS - 1)
                i1 = sp.value_load(idx[0:1, bass.ds(b + B, 1)], min_val=0, max_val=SLOTS - 1)
                sp.dma_start(stage_w(LORA_ITEM, 0)[:, bass.ds(b * BR, BR)],
                             A1T[bass.ds(i1, 1), :, :, :].rearrange("s p k r -> p (s k r)")).then_inc(lora_landed, DMA)
                sp.dma_start(stage_w(LORA_ITEM, 1)[:, bass.ds(b * BR, BR)],
                             B0T[bass.ds(i0, 1), :, :, :].rearrange("s p k r -> p (s k r)")).then_inc(lora_landed, DMA)
            for i in range(LORA_ITEM + 1, len(items)):
                load_w(i, items[i][1])
            for b in range(B):
                i1 = sp.value_load(idx[0:1, B + b:B + b + 1], min_val=0, max_val=SLOTS - 1)
                sp.dma_start(b1_raw[b * RK:(b + 1) * RK, :],
                             B1[bass.ds(i1, 1), :, :].rearrange("s r n -> (s r) n")).then_inc(b1_landed, DMA)
            sp.wait_ge(bias_zeroed, 1)
            sp.dma_start(bias_sum[0:1, :], b1).then_inc(bias1_landed, DMA)
            stage_consumed(sp, LORA_ITEM)
            load_x(0, 0)
            load_a0(0, 0)
            stage_consumed(sp, LORA_ITEM + 1)
            load_x(1, 1)
            load_a0(1, 1)
            def words(v):
                return v.bitcast(F32)

            sp.wait_ge(rc_lo, 3 * NH)
            for b in range(B):
                for g, part in enumerate((0, 1, 0)):
                    for j, src in enumerate((r_hl, b1_hl)):
                        r0 = (2 * g + j) * RK
                        sp.dma_start(words(rb[r0:r0 + RK, b, :]), words(src[b * RK:(b + 1) * RK, part, :])).then_inc(rb_landed, DMA)
            for part in range(2):
                sp.dma_start(words(rb[6 * RK + part:6 * RK + part + 1, :, :]), words(c_hl[:, part, :])).then_inc(rb_landed, DMA)
            with sp.Fori(1, B // 2) as i:
                for s in range(2):
                    sp.wait_ge(x_ready, i * 2 + (s - 1))
                    load_x(s, i * 2 + s)
                    load_a0(s, i * 2 + s, i * 2 + (s - 1))
        RB_DMAS = 6 * B + 2

        @block.gpsimd
        def _(pool):
            nc.gpsimd.memset(ident[:, :], 0.0).then_inc(ident_made, 1)
            pool.wait_ge(ident_made, 1)
            nc.gpsimd.affine_select(out=ident[:, :], in_=ident[:, :], compare_op=ALU.not_equal, fill=1.0, base=0,
                                    pattern=[[-1, P]], channel_multiplier=1).then_inc(ident_made, 1)
            nc.gpsimd.memset(ones_b[:, :], 1.0)
            nc.gpsimd.memset(same_batch[:, :, :], 1.0).then_inc(masks_made, 1)
            pool.wait_ge(masks_made, 1)
            nc.gpsimd.affine_select(out=same_batch[:, :, :], in_=same_batch[:, :, :], compare_op=ALU.is_ge, fill=0.0,
                                    base=0, pattern=[[-RK, B], [0, RK]], channel_multiplier=1).then_inc(masks_made, 1)
            pool.wait_ge(masks_made, 2)
            nc.gpsimd.affine_select(out=same_batch[:, :, :], in_=same_batch[:, :, :], compare_op=ALU.is_ge, fill=0.0,
                                    base=RK - 1, pattern=[[RK, B], [0, RK]], channel_multiplier=-1
                                    ).then_inc(masks_made, 1)

        @block.scalar
        def _(act):
            def high_w(i):
                k, n, s = items[i][1], weights_to[i], i % STAGE_SLOTS
                act.wait_ge(diag_added, 2 * n - 1)
                nc.scalar.copy(w0_hi[:, :, k * P:(k + 1) * P],
                               stage_w(i, 0).rearrange("p (m c) -> p m c", m=KT)).then_inc(hi_made, 1)
                act.wait_ge(diag_added, 2 * n)
                nc.scalar.copy(w1_hi[:, k, :], stage_w(i, 1)).then_inc(hi_made, 1)

            def high_lora():
                act.wait_ge(lora_landed, 2 * B * DMA)
                for which, to in ((0, a1), (1, b0w)):
                    nc.scalar.copy(to[:, :, 0:BR].rearrange("p k (b r) -> p b k r", b=B),
                                   stage_w(LORA_ITEM, which).rearrange("p (b k r) -> p b k r", b=B, k=KT)
                                   ).then_inc(lora_hi, 1)
                act.wait_ge(b0_landed, DMA)
                nc.scalar.copy(b0w[:, :, 2 * BR], b0_raw[:, :]).then_inc(lora_hi, 1)

            def aux_copy(j):
                act.wait_ge(aux_summed, j + 1)
                if j >= 1:
                    act.wait_ge(aux_done, j)
                n = 2 * BR + 2 if j == AUX_ST else BR
                nc.scalar.copy(scratch[:, 0:n], banks[6 + j % 2][:, 0:n]).then_inc(aux_copied, 1)

            def high_d(m):
                if m >= FIRST_M:
                    act.wait_ge(d_summed, NH * (m - FIRST_M + 1))
                for h in range(NH):
                    nc.scalar.copy(w0_hi[:, m, h * HALF:(h + 1) * HALF], banks[(NH * m + h) % BANKS_D][:, :]
                                   ).then_inc(d_hi, 1)

            for i in range(len(items)):
                if items[i][0] == "w":
                    high_w(i)
                else:
                    high_lora()
            for m in range(FIRST_M):
                aux_copy(m)
                high_d(m)
            aux_copy(AUX_ST)
            for m in range(FIRST_M, KT):
                aux_copy(m + 1)
                high_d(m)
            for h in range(NH):
                act.wait_ge(r_summed, h + 1)
                nc.scalar.mul(r_hl[:, 0, h * HALF:(h + 1) * HALF], banks[(NH * KT + h) % BANKS_D][:, :], 2.0
                              ).then_inc(rc_hi, 1)
            act.wait_ge(b1_landed, B * DMA)
            for h in range(NH):
                nc.scalar.copy(b1_hl[:, 0, h * HALF:(h + 1) * HALF], b1_raw[:, h * HALF:(h + 1) * HALF]
                               ).then_inc(rc_hi, 1)
            for h in range(NH):
                act.wait_ge(c_summed, h + 1)
                nc.scalar.copy(c_hl[:, 0, h * HALF:(h + 1) * HALF],
                               banks[(NH * (KT + 1) + h) % BANKS_D][0:B, :]).then_inc(rc_hi, 1)

            act.wait_ge(rc_lo, 3 * NH)

            def put(i, n, first):
                per = 2 * QT * NH
                act.wait_ge(out_summed, i * per + n + 1)
                if not first or n >= 4:
                    act.wait_ge(stored[n % 4], (i * (per // 4) + n // 4) * DMA)
                nc.scalar.copy(rows[:, n % 4, :], banks[(n + 2) % 4][:, :]).then_inc(out_copied, 1)
                act.wait_ge(out_copied, i * per + n + 1)
                t, h = n // NH, n % NH
                act.dma_start(out[bass.ds(i * (2 * T) + t * P, P), h * HALF:(h + 1) * HALF], rows[:, n % 4, :]
                              ).then_inc(stored[n % 4], DMA)

            for n in range(2 * QT * NH):
                put(0, n, True)
            with act.Fori(1, B // 2) as i:
                for n in range(2 * QT * NH):
                    put(i, n, False)
            for s in range(4):
                act.wait_ge(stored[s], B * QT * NH // 4 * DMA)

        @block.vector
        def _(dve):
            def low_w(i):
                k, n, s = items[i][1], weights_to[i], i % STAGE_SLOTS
                for which, landed in ((0, w0_landed), (1, w1_landed)):
                    dve.wait_ge(landed[s], slot_uses[i] * DMA)
                    if i == 0 and which == 0:
                        dve.wait_ge(ident_made, 2)
                    block_k = stage_w(i, which)[:, k * P:(k + 1) * P]
                    nc.vector.tensor_tensor(block_k, block_k, ident[:, :], ALU.add).then_inc(diag_added, 1)
                dve.wait_ge(hi_made, 2 * n - 1)
                nc.vector.tensor_tensor(w0_lo[:, :, k * P:(k + 1) * P],
                                        stage_w(i, 0).rearrange("p (m c) -> p m c", m=KT),
                                        w0_hi[:, :, k * P:(k + 1) * P], ALU.subtract).then_inc(lo_made, 1)
                dve.wait_ge(hi_made, 2 * n)
                nc.vector.tensor_tensor(w1_lo[:, k, :], stage_w(i, 1), w1_hi[:, k, :], ALU.subtract
                                        ).then_inc(lo_made, 1)

            def low_lora():
                for n, (which, to) in enumerate(((0, a1), (1, b0w))):
                    dve.wait_ge(lora_hi, n + 1)
                    nc.vector.tensor_tensor(to[:, :, BR:2 * BR].rearrange("p k (b r) -> p b k r", b=B),
                                            stage_w(LORA_ITEM, which).rearrange("p (b k r) -> p b k r", b=B, k=KT),
                                            to[:, :, 0:BR].rearrange("p k (b r) -> p b k r", b=B),
                                            ALU.subtract).then_inc(lora_lo, 1)
                dve.wait_ge(lora_hi, 3)
                nc.vector.tensor_tensor(b0w[:, :, 2 * BR + 1], b0_raw[:, :], b0w[:, :, 2 * BR],
                                        ALU.subtract).then_inc(lora_lo, 1)

            def g_add(m, j):
                dve.wait_ge(aux_copied, j + 1)
                nc.vector.tensor_tensor(g_all[:, m, :], banks[6 + j % 2][:, BR:2 * BR], scratch[:, 0:BR],
                                        ALU.add).then_inc(aux_done, 1)

            def low_d(m):
                for h in range(NH):
                    dve.wait_ge(d_hi, NH * m + h + 1)
                    cols = slice(h * HALF, (h + 1) * HALF)
                    nc.vector.tensor_tensor(w0_lo[:, m, cols], banks[(NH * m + h) % BANKS_D][:, :],
                                            w0_hi[:, m, cols], ALU.subtract).then_inc(d_lo, 1)

            def bias_add(k):
                for n, part in enumerate((w1_hi, w1_lo)):
                    if 2 * k + n == 0:
                        dve.wait_ge(bias1_landed, DMA)
                    else:
                        dve.wait_ge(bias_step, 2 * k + n)
                    nc.vector.scalar_tensor_tensor(out=bias_sum, in0=part[:, k, :], scalar=b0_raw[:, k:k + 1],
                                                   in1=bias_sum, op0=ALU.mult, op1=ALU.add).then_inc(bias_step, 1)


            def split_x(i, s, first=False):
                b = i * 2 + s
                dve.wait_ge(x_landed[s], (i + 1) * DMA)
                if not first:
                    dve.wait_ge(out_summed, (b - 1) * (QT * NH))
                raw = stage[:, s, :].rearrange("p (k t) -> p k t", k=KT)
                nc.vector.tensor_copy(x_hi[s], raw).then_inc(x_hi_made, 1)
                dve.wait_ge(x_hi_made, b + 1)
                nc.vector.tensor_tensor(x_lo[s], raw, x_hi[s], ALU.subtract).then_inc(x_ready, 1)

            def factors(i, s, first=False):
                b = i * 2 + s
                to = aa[:, s, 0:KT * 4 * RK].rearrange("p (k c) -> p k c", k=KT)
                g = g_all[:, :, bass.ds(b * RK, RK)]
                a0 = a0_raw[:, s, :].rearrange("p (k r) -> p k r", k=KT)
                dve.wait_ge(a0_landed[s], (i + 1) * DMA)
                if not first:
                    dve.wait_ge(h_summed, b - 1)
                nc.vector.tensor_copy(to[:, :, 0:RK], a0).then_inc(aa_hi, 1)
                nc.vector.tensor_copy(to[:, :, RK:2 * RK], g).then_inc(aa_hi, 1)
                dve.wait_ge(aa_hi, b * 2 + 2)
                nc.vector.tensor_tensor(to[:, :, 3 * RK:4 * RK], g, to[:, :, RK:2 * RK], ALU.subtract)
                nc.vector.tensor_tensor(to[:, :, 2 * RK:3 * RK], a0, to[:, :, 0:RK], ALU.subtract).then_inc(aa_ready, 1)

            def stack_h(i, s):
                b = i * 2 + s
                bank = banks[6 + s]
                dve.wait_ge(h_summed, b + 1)
                nc.vector.tensor_copy(h_tmp, bank[2 * RK:4 * RK, 0:T]).then_inc(h_moved, 1)
                dve.wait_ge(h_moved, b + 1)
                nc.vector.tensor_tensor(h_sum[:, :], bank[0:2 * RK, 0:T], h_tmp, ALU.add).then_inc(h_added, 1)
                dve.wait_ge(h_added, b + 1)
                nc.vector.tensor_copy(h_stack[s][0:2 * RK, :], h_sum[:, :]).then_inc(h_hi, 1)
                nc.vector.tensor_copy(h_stack[s][2 * RK:4 * RK, :], h_sum[:, :]).then_inc(h_hi, 1)
                dve.wait_ge(h_hi, b * 2 + 2)
                nc.vector.tensor_tensor(h_stack[s][4 * RK:6 * RK, :], h_sum[:, :], h_stack[s][0:2 * RK, :],
                                        ALU.subtract).then_inc(h_ready, 1)

            nc.vector.memset(bias_sum, 0.0).then_inc(bias_zeroed, 1)
            for s in range(2):
                nc.vector.memset(aa[:, s, KT * 4 * RK:AA_W].bitcast(F32), 0.0).then_inc(pad_set, 1)
            for i in range(len(items)):
                if items[i][0] == "w":
                    low_w(i)
                else:
                    low_lora()
            for m in range(FIRST_M):
                g_add(m, m)
                low_d(m)
            dve.wait_ge(aux_copied, AUX_ST + 1)
            dve.wait_ge(masks_made, 3)
            nc.vector.tensor_tensor(s_t[:, :], scratch[:, 0:BR], scratch[:, BR:2 * BR], ALU.add).then_inc(st_step, 1)
            nc.vector.tensor_tensor(t_sum[:, :], scratch[:, 2 * BR:2 * BR + 1], scratch[:, 2 * BR + 1:2 * BR + 2],
                                    ALU.add).then_inc(aux_done, 1)
            dve.wait_ge(st_step, 1)
            nc.vector.tensor_tensor(s_t[:, :], s_t[:, :], same_batch[:, :, :].rearrange("p b r -> p (b r)"),
                                    ALU.mult).then_inc(st_step, 1)
            dve.wait_ge(aux_done, AUX_ST + 1)
            nc.vector.tensor_scalar(t_blk[:, :], same_batch[:, :, 0], t_sum[:, 0:1], None, ALU.mult
                                    ).then_inc(st_step, 1)
            for m in range(FIRST_M, KT):
                g_add(m, m + 1)
                if m < KT - 1:
                    for k in range(2 * (m - FIRST_M), 2 * (m - FIRST_M) + 2):
                        bias_add(k)
                else:
                    split_x(0, 0, True)
                    factors(0, 0, True)
                low_d(m)
            for h in range(NH):
                cols = slice(h * HALF, (h + 1) * HALF)
                dve.wait_ge(rc_hi, h + 1)
                nc.vector.scalar_tensor_tensor(out=r_hl[:, 1, cols], in0=banks[(NH * KT + h) % BANKS_D][:, :],
                                               scalar=2.0, in1=r_hl[:, 0, cols], op0=ALU.mult, op1=ALU.subtract
                                               ).then_inc(rc_lo, 1)
            for h in range(NH):
                cols = slice(h * HALF, (h + 1) * HALF)
                dve.wait_ge(rc_hi, NH + h + 1)
                nc.vector.tensor_tensor(b1_hl[:, 1, cols], b1_raw[:, cols], b1_hl[:, 0, cols], ALU.subtract
                                        ).then_inc(rc_lo, 1)
            for h in range(NH):
                cols = slice(h * HALF, (h + 1) * HALF)
                dve.wait_ge(rc_hi, 2 * NH + h + 1)
                nc.vector.tensor_tensor(c_hl[:, 1, cols], banks[(NH * (KT + 1) + h) % BANKS_D][0:B, :],
                                        c_hl[:, 0, cols], ALU.subtract).then_inc(rc_lo, 1)
            for s in range(2):
                nc.vector.memset(h_stack[s][6 * RK:6 * RK + 2, :].bitcast(F32), 1.0).then_inc(ones_set, 1)

            stack_h(0, 0)
            split_x(0, 1, True)
            factors(0, 1, True)
            stack_h(0, 1)
            with dve.Fori(1, B // 2) as i:
                for s in range(2):
                    split_x(i, s)
                    factors(i, s)
                    stack_h(i, s)

        @block.tensor
        def _(pe):
            mm = nc.tensor.matmul

            def d_pass(m, h, k, left, right, start, stop):
                return mm(banks[(NH * m + h) % BANKS_D][:, :], left[:, m, k * P:(k + 1) * P],
                          right[:, k, h * HALF:(h + 1) * HALF], start=start, stop=stop)

            def aux(j, m):
                if j >= 2:
                    pe.wait_ge(aux_done, j - 1)
                for k in range(KT):
                    for n, left in enumerate((w0_hi, w0_lo)):
                        last = mm(banks[6 + j % 2][:, 0:2 * BR], left[:, m, k * P:(k + 1) * P], a1[:, k, :],
                                  start=(k == 0 and n == 0), stop=(k == KT - 1 and n == 1))
                last.then_inc(aux_summed, 1)

            for k in range(KT):
                pe.wait_ge(hi_made, 2 * k + 2)
                for m in range(FIRST_M):
                    for h in range(NH):
                        d_pass(m, h, k, w0_hi, w1_hi, k == 0, False)
                pe.wait_ge(lo_made, 2 * k + 2)
                for m in range(FIRST_M):
                    for h in range(NH):
                        d_pass(m, h, k, w0_hi, w1_lo, False, False)
                        d_pass(m, h, k, w0_lo, w1_hi, False, k == KT - 1)
            pe.wait_ge(lora_lo, 3)
            for m in range(FIRST_M):
                aux(m, m)
            pe.wait_ge(aux_done, AUX_ST - 1)
            for k in range(KT):
                for n in range(2):
                    last = mm(banks[6 + AUX_ST % 2][:, 0:2 * BR + 2], a1[:, k, n * BR:(n + 1) * BR], b0w[:, k, :],
                              start=(k == 0 and n == 0), stop=(k == KT - 1 and n == 1))
            last.then_inc(aux_summed, 1)
            for m in range(FIRST_M, KT):
                aux(m + 1, m)
                for h in range(NH):
                    pe.wait_ge(d_lo, NH * m + h + 1 - BANKS_D)
                    for k in range(KT):
                        d_pass(m, h, k, w0_hi, w1_hi, k == 0, False)
                        d_pass(m, h, k, w0_hi, w1_lo, False, False)
                        last = d_pass(m, h, k, w0_lo, w1_hi, False, k == KT - 1)
                    last.then_inc(d_summed, 1)
            pe.wait_ge(st_step, 3)
            pe.wait_ge(b1_landed, B * DMA)
            for h in range(NH):
                cols = slice(h * HALF, (h + 1) * HALF)
                bank = banks[(NH * KT + h) % BANKS_D]
                pe.wait_ge(d_lo, NH * KT + h + 1 - BANKS_D)
                mm(bank[:, :], s_t[:, :], b1_raw[:, cols], start=True, stop=False)
                for k in range(KT):
                    hi, lo = b0w[:, k, 0:BR], b0w[:, k, BR:2 * BR]
                    mm(bank[:, :], hi, w1_hi[:, k, cols], start=False, stop=False)
                    mm(bank[:, :], hi, w1_lo[:, k, cols], start=False, stop=False)
                    last = mm(bank[:, :], lo, w1_hi[:, k, cols], start=False, stop=(k == KT - 1))
                last.then_inc(r_summed, 1)
            pe.wait_ge(bias_step, 2 * KT)
            for h in range(NH):
                cols = slice(h * HALF, (h + 1) * HALF)
                bank = banks[(NH * (KT + 1) + h) % BANKS_D]
                pe.wait_ge(d_lo, NH * (KT + 1) + h + 1 - BANKS_D)
                mm(bank[0:B, :], ones_b[:, :], bias_sum[:, cols], start=True, stop=False)
                mm(bank[0:B, :], t_blk[:, :], b1_raw[:, cols], start=False, stop=True).then_inc(c_summed, 1)

            def batch(i, s, first):
                b = i * 2 + s
                pe.wait_ge(x_ready, b + 1)
                pe.wait_ge(aa_ready, b + 1)
                if not first:
                    pe.wait_ge(h_added, b - 1)
                for k in range(KT):
                    for n, part in enumerate((x_hi[s], x_lo[s])):
                        last = mm(banks[6 + s][:, 0:T], aa[:, s, k * 4 * RK:k * 4 * RK + P], part[:, k, :],
                                  start=(k == 0 and n == 0), stop=(k == KT - 1 and n == 1))
                last.then_inc(h_summed, 1)
                for q in range(QT):
                    tok = slice(q * P, (q + 1) * P)
                    for h in range(NH):
                        n = (s * QT + q) * NH + h
                        cols = slice(h * HALF, (h + 1) * HALF)
                        bank = banks[(n + 2) % 4][:, :]
                        if not (first and n < 4):
                            pe.wait_ge(out_copied, i * (2 * QT * NH) + (n - 3))
                        for k in range(KT):
                            mm(bank, x_hi[s][:, k, tok], w0_hi[:, k, cols], start=(k == 0), stop=False)
                            mm(bank, x_hi[s][:, k, tok], w0_lo[:, k, cols], start=False, stop=False)
                            mm(bank, x_lo[s][:, k, tok], w0_hi[:, k, cols], start=False, stop=False)
                        if q == 0 and h == 0:
                            pe.wait_ge(h_ready, b + 1)
                            if first and s == 0:
                                pe.wait_ge(rb_landed, RB_DMAS * DMA)
                                pe.wait_ge(ones_set, 2)
                        mm(bank, h_stack[s][0:STACK, tok], w1[0:STACK, bass.ds(b * D + h * HALF, HALF)], start=False, stop=True
                           ).then_inc(out_summed, 1)

            pe.wait_ge(d_lo, NH * KT)
            pe.wait_ge(pad_set, 2)
            for s in range(2):
                batch(0, s, True)
            with pe.Fori(1, B // 2) as i:
                for s in range(2):
                    batch(i, s, False)


def kernel(x, itok_B_0_23, itok_B_6_15, L0_cond_W, L0_cond_b, L0_cond_lora_As, L0_cond_lora_Bs,
           L1_cond_base_weight, L1_cond_base_bias, L1_cond_lora_A_w, L1_cond_lora_B_w):
    import numpy as np
    import concourse.bacc as bacc
    from concourse.bass_utils import run_bass_kernel_spmd

    x = np.asarray(x)
    B, T, D = x.shape
    kt = D // P

    def by_partition(a, axis):
        a = np.asarray(a)
        a = np.moveaxis(a, axis, 1)
        a = a.reshape(a.shape[0], kt, P, *a.shape[2:])
        return np.moveaxis(a, 2, 1)

    ins = {
        "xT": by_partition(x, 2),
        "W0": np.asarray(L0_cond_W),
        "W1T": np.asarray(L1_cond_base_weight).T,
        "A0": by_partition(L0_cond_lora_As, 1),
        "B0T": by_partition(L0_cond_lora_Bs, 2),
        "A1T": by_partition(L1_cond_lora_A_w, 2),
        "B1": np.asarray(L1_cond_lora_B_w).transpose(0, 2, 1),
        "b0": np.asarray(L0_cond_b).reshape(kt, P).T,
        "b1": np.asarray(L1_cond_base_bias).reshape(1, D),
        "idx0": np.asarray(itok_B_0_23).reshape(1, B),
        "idx1": np.asarray(itok_B_6_15).reshape(1, B),
    }
    nc = bacc.Bacc("TRN2", target_bir_lowering=False, num_devices=1)
    arrays, args = {}, []
    for name, a in ins.items():
        a = np.ascontiguousarray(a)
        arrays[name] = a
        args.append(nc.dram_tensor(name, a.shape, mybir.dt.from_np(a.dtype), kind="ExternalInput").ap())
    out = nc.dram_tensor("out", (B * T, D), F32, kind="ExternalOutput").ap()
    lora_pair(nc, *args, out)
    r = run_bass_kernel_spmd(nc, [arrays], core_ids=[0])
    return r.results[0]["out"].reshape(B, T, D)
```

```python
from contextlib import ExitStack

import concourse.bass as bass
from concourse import mybir

F32 = mybir.dt.float32
F32R = mybir.dt.float32r
I32 = mybir.dt.int32
ALU = mybir.AluOpType
ACT = mybir.ActivationFunctionType

P = 128
HALF = 512
STAGE_SLOTS = 3
BANKS_D = 6
FIRST_M = 3
DMA = 16


def lora_pair(nc, xT, W0, W1T, A0, B0T, A1T, B1, b0, b1, idx0, idx1, out):
    B, _, KT, T = xT.shape
    D = KT * P
    NH = D // HALF
    RK = A0.shape[-1]
    SLOTS = A0.shape[0]
    BR = B * RK
    assert BR == P and NH == 2 and T == 2 * P and B % 2 == 0
    QT = T // P
    STACK = 6 * RK + 2
    AUX_ST = FIRST_M

    with ExitStack() as ctx:
        def sb(name, shape, dt):
            return ctx.enter_context(nc.sbuf_tensor(name, shape, dt))

        def sem(name):
            return ctx.enter_context(nc.semaphore(name))

        w0_hi = sb("w0_hi", [P, KT, D], F32R)
        w0_lo = sb("w0_lo", [P, KT, D], F32R)
        w1 = sb("w1", [P, 2 * KT * D], F32R)
        w1_hi = w1[:, 0:KT * D].rearrange("p (k n) -> p k n", k=KT)
        w1_lo = w1[:, KT * D:2 * KT * D].rearrange("p (k n) -> p k n", k=KT)
        stage = sb("stage", [P, STAGE_SLOTS, 2 * D], F32)
        a1 = sb("a1", [P, KT, 2 * BR], F32R)
        b0w = sb("b0w", [P, KT, 2 * BR + 2], F32R)
        g_all = sb("g_all", [P, KT, BR], F32)
        AA_W = KT * 4 * RK + 4 * RK
        aa = sb("aa", [P, 2, AA_W], F32R)
        a0_raw = sb("a0_raw", [P, 2, KT * RK], F32)
        x_first = sb("x_first", [P, 2, KT * T], F32R)
        rows = sb("rows", [P, 4, HALF], F32)
        bias_sum = rows[:, 0:2, :].rearrange("p a n -> p (a n)")
        b1_raw = rows[:, 2:4, :].rearrange("p a n -> p (a n)")
        scratch = sb("scratch", [P, 2 * BR + 2], F32)
        s_t = sb("s_t", [P, BR], F32)
        h_sum = sb("h_sum", [2 * RK, T], F32)
        t_blk = sb("t_blk", [P, B], F32)
        ident = sb("ident", [P, P], F32)
        same_batch = sb("same_batch", [P, B, RK], F32)
        ones_b = sb("ones_b", [P, B], F32)
        b0_raw = sb("b0_raw", [P, KT], F32)
        t_sum = sb("t_sum", [P, 1], F32)
        r_dram = nc.dram_tensor("r_rows", (BR, 2, D), F32, kind="Internal").ap()
        b1_dram = nc.dram_tensor("b1_rows", (BR, 2, D), F32, kind="Internal").ap()
        idx = sb("idx", [1, 2 * B], I32)

        rb = w1[0:STACK, 0:B * D].rearrange("p (b n) -> p b n", b=B)
        at = B * D
        x_second = w1[:, at:at + 2 * KT * T].rearrange("p (s n) -> p s n", s=2)
        at += 2 * KT * T
        h_stack = [w1[:, at + s * T:at + (s + 1) * T] for s in range(2)]
        at += 2 * T
        c_hl = w1[0:B, at:at + 2 * D].rearrange("p (s n) -> p s n", s=2)
        at += 2 * D
        assert at <= 2 * KT * D
        x_hi = [v[:, 0, :].rearrange("p (k t) -> p k t", k=KT) for v in (x_first, x_second)]
        x_lo = [v[:, 1, :].rearrange("p (k t) -> p k t", k=KT) for v in (x_first, x_second)]
        r_hl = a1[:, :, :].rearrange("p k n -> p (k n)").rearrange("p (s n) -> p s n", s=2)
        b1_hl = b0w[:, :, :].rearrange("p k n -> p (k n)")[:, 0:2 * D].rearrange("p (s n) -> p s n", s=2)

        banks = [ctx.enter_context(nc.psum_tensor(f"bank{i}", [P, HALF], F32)) for i in range(8)]
        h_tmp = scratch[0:32, 0:T]

        w0_landed = [sem(f"w0_landed{s}") for s in range(STAGE_SLOTS)]
        w1_landed = [sem(f"w1_landed{s}") for s in range(STAGE_SLOTS)]
        lora_landed = sem("lora_landed")
        b1_landed = sem("b1_landed")
        idx_landed = sem("idx_landed")
        b0_landed = sem("b0_landed")
        bias1_landed = sem("bias1_landed")
        x_landed = [sem(f"x_landed{s}") for s in range(2)]
        a0_landed = [sem(f"a0_landed{s}") for s in range(2)]
        bounced = [sem("r_bounced"), sem("b1_bounced")]
        rb_landed = sem("rb_landed")
        stored = [sem(f"stored{s}") for s in range(4)]
        ident_made = sem("ident_made")
        masks_made = sem("masks_made")
        bias_zeroed = sem("bias_zeroed")
        diag_added = sem("diag_added")
        hi_made = sem("hi_made")
        lo_made = sem("lo_made")
        lora_hi = sem("lora_hi")
        lora_lo = sem("lora_lo")
        d_summed = sem("d_summed")
        d_hi = sem("d_hi")
        d_lo = sem("d_lo")
        aux_summed = sem("aux_summed")
        aux_copied = sem("aux_copied")
        aux_done = sem("aux_done")
        bias_step = sem("bias_step")
        st_step = sem("st_step")
        r_summed = sem("r_summed")
        c_summed = sem("c_summed")
        rc_hi = sem("rc_hi")
        b1_hi_made = sem("b1_hi_made")
        rc_lo = sem("rc_lo")
        ones_set = sem("ones_set")
        pad_set = sem("pad_set")
        aa_hi = sem("aa_hi")
        aa_ready = sem("aa_ready")
        x_hi_made = sem("x_hi_made")
        x_ready = sem("x_ready")
        h_summed = sem("h_summed")
        h_moved = sem("h_moved")
        h_added = sem("h_added")
        h_hi = sem("h_hi")
        h_ready = sem("h_ready")
        out_summed = sem("out_summed")
        out_copied = sem("out_copied")

        block = ctx.enter_context(nc.Block())

        LORA_AFTER = 6
        a1_raw = g_all[:, :, :].rearrange("p k n -> p (k n)")
        b0t_raw = b1_raw

        def slot_uses(k):
            return k // STAGE_SLOTS + 1

        def stage_w(k, which):
            return stage[:, k % STAGE_SLOTS, which * D:(which + 1) * D]

        def words(v):
            return v.bitcast(F32)

        @block.sync
        def _(sp):
            def load_x(s, b):
                sp.dma_start(stage[:, s, :], xT[bass.ds(b, 1), :, :, :].rearrange("b p k t -> p (b k t)")
                             ).then_inc(x_landed[s], DMA)

            for k in range(KT):
                s = k % STAGE_SLOTS
                if k >= STAGE_SLOTS:
                    sp.wait_ge(lo_made, 2 * (k - STAGE_SLOTS + 1))
                sp.dma_start(stage_w(k, 0), W0[k * P:(k + 1) * P, :]).then_inc(w0_landed[s], DMA)
                sp.dma_start(stage_w(k, 1), W1T[k * P:(k + 1) * P, :]).then_inc(w1_landed[s], DMA)
                if k == 0:
                    sp.dma_start(idx[0:1, 0:B], idx0).then_inc(idx_landed, DMA)
                    sp.dma_start(idx[0:1, B:2 * B], idx1).then_inc(idx_landed, DMA)
                    sp.dma_start(b0_raw[:, :], b0).then_inc(b0_landed, DMA)
            sp.wait_ge(bias_zeroed, 1)
            sp.dma_start(bias_sum[0:1, :], b1).then_inc(bias1_landed, DMA)
            for s in range(2):
                last_tile = (KT - 1) // STAGE_SLOTS * STAGE_SLOTS + s
                sp.wait_ge(lo_made, 2 * (last_tile + 1))
                load_x(s, s)
            for n, (src, via) in enumerate(((r_hl, r_dram), (b1_hl, b1_dram))):
                sp.wait_ge(rc_lo, NH * (n + 1))
                sp.dma_start(via, words(src)).then_inc(bounced[n], DMA)
            sp.wait_ge(rc_lo, 3 * NH)
            for part in range(2):
                sp.dma_start(words(rb[6 * RK + part:6 * RK + part + 1, :, :]), words(c_hl[:, part, :])
                             ).then_inc(rb_landed, DMA)
            for n, via in enumerate((r_dram, b1_dram)):
                sp.wait_ge(bounced[n], DMA)
                for g, part in enumerate((0, 1, 0)):
                    r0 = (2 * g + n) * RK
                    sp.dma_start(words(rb[r0:r0 + RK, :, :]), via[:, part, :].rearrange("(b r) n -> r b n", b=B)
                                 ).then_inc(rb_landed, DMA)
            with sp.Fori(1, B // 2) as i:
                for s in range(2):
                    sp.wait_ge(x_ready, i * 2 + (s - 1))
                    load_x(s, i * 2 + s)
        RB_DMAS = 6 + 2

        @block.gpsimd
        def _(pool):
            nc.gpsimd.memset(ident[:, :], 0.0).then_inc(ident_made, 1)
            pool.wait_ge(ident_made, 1)
            nc.gpsimd.affine_select(out=ident[:, :], in_=ident[:, :], compare_op=ALU.not_equal, fill=1.0, base=0,
                                    pattern=[[-1, P]], channel_multiplier=1).then_inc(ident_made, 1)
            nc.gpsimd.memset(ones_b[:, :], 1.0)
            nc.gpsimd.memset(same_batch[:, :, :], 1.0).then_inc(masks_made, 1)
            pool.wait_ge(masks_made, 1)
            nc.gpsimd.affine_select(out=same_batch[:, :, :], in_=same_batch[:, :, :], compare_op=ALU.is_ge, fill=0.0,
                                    base=0, pattern=[[-RK, B], [0, RK]], channel_multiplier=1).then_inc(masks_made, 1)
            pool.wait_ge(masks_made, 2)
            nc.gpsimd.affine_select(out=same_batch[:, :, :], in_=same_batch[:, :, :], compare_op=ALU.is_ge, fill=0.0,
                                    base=RK - 1, pattern=[[RK, B], [0, RK]], channel_multiplier=-1
                                    ).then_inc(masks_made, 1)

            def adapter(b):
                return pool.value_load(idx[0:1, bass.ds(b, 1)], min_val=0, max_val=SLOTS - 1)

            pool.wait_ge(idx_landed, 2 * DMA)
            with pool.Fori(0, B) as b:
                i0, i1 = adapter(b), adapter(b + B)
                pool.dma_start(a1_raw[:, bass.ds(b * BR, BR)],
                               A1T[bass.ds(i1, 1), :, :, :].rearrange("s p k r -> p (s k r)")).then_inc(lora_landed, DMA)
                pool.dma_start(b0t_raw[:, bass.ds(b * BR, BR)],
                               B0T[bass.ds(i0, 1), :, :, :].rearrange("s p k r -> p (s k r)")).then_inc(lora_landed, DMA)

            def load_a0(s, b, free=None):
                i0 = adapter(b)
                if free is not None:
                    pool.wait_ge(aa_ready, free)
                pool.dma_start(a0_raw[:, s, :], A0[bass.ds(i0, 1), :, :, :].rearrange("s p k r -> p (s k r)")
                               ).then_inc(a0_landed[s], DMA)

            for s in range(2):
                load_a0(s, s)
            pool.wait_ge(lora_lo, 3)
            for b in range(B):
                i1 = adapter(B + b)
                pool.dma_start(b1_raw[b * RK:(b + 1) * RK, :],
                               B1[bass.ds(i1, 1), :, :].rearrange("s r n -> (s r) n")).then_inc(b1_landed, DMA)
            with pool.Fori(1, B // 2) as i:
                for s in range(2):
                    load_a0(s, i * 2 + s, i * 2 + (s - 1))

        @block.scalar
        def _(act):
            def high_w(k):
                act.wait_ge(diag_added, 2 * k + 1)
                nc.scalar.copy(w0_hi[:, :, k * P:(k + 1) * P],
                               stage_w(k, 0).rearrange("p (m c) -> p m c", m=KT)).then_inc(hi_made, 1)
                act.wait_ge(diag_added, 2 * k + 2)
                nc.scalar.copy(w1_hi[:, k, :], stage_w(k, 1)).then_inc(hi_made, 1)

            def high_lora():
                act.wait_ge(lora_landed, 2 * B * DMA)
                for raw, to in ((a1_raw, a1), (b0t_raw, b0w)):
                    nc.scalar.copy(to[:, :, 0:BR].rearrange("p k (b r) -> p b k r", b=B),
                                   raw.rearrange("p (b k r) -> p b k r", b=B, k=KT)).then_inc(lora_hi, 1)
                act.wait_ge(b0_landed, DMA)
                nc.scalar.copy(b0w[:, :, 2 * BR], b0_raw[:, :]).then_inc(lora_hi, 1)

            def aux_copy(j):
                act.wait_ge(aux_summed, j + 1)
                if j >= 1:
                    act.wait_ge(aux_done, j)
                n = 2 * BR + 2 if j == AUX_ST else BR
                nc.scalar.copy(scratch[:, 0:n], banks[6 + j % 2][:, 0:n]).then_inc(aux_copied, 1)

            def high_d(m):
                if m >= FIRST_M:
                    act.wait_ge(d_summed, NH * (m - FIRST_M + 1))
                for h in range(NH):
                    nc.scalar.copy(w0_hi[:, m, h * HALF:(h + 1) * HALF], banks[(NH * m + h) % BANKS_D][:, :]
                                   ).then_inc(d_hi, 1)

            for k in range(KT):
                high_w(k)
                if k == LORA_AFTER:
                    high_lora()
            for m in range(FIRST_M):
                aux_copy(m)
                high_d(m)
            aux_copy(AUX_ST)
            for m in range(FIRST_M, KT):
                aux_copy(m + 1)
                high_d(m)
            for h in range(NH):
                act.wait_ge(r_summed, h + 1)
                nc.scalar.mul(r_hl[:, 0, h * HALF:(h + 1) * HALF], banks[(NH * KT + h) % BANKS_D][:, :], 2.0
                              ).then_inc(rc_hi, 1)
            act.wait_ge(b1_landed, B * DMA)
            for h in range(NH):
                nc.scalar.copy(b1_hl[:, 0, h * HALF:(h + 1) * HALF], b1_raw[:, h * HALF:(h + 1) * HALF]
                               ).then_inc(rc_hi, 1)
            for h in range(NH):
                act.wait_ge(c_summed, h + 1)
                nc.scalar.copy(c_hl[:, 0, h * HALF:(h + 1) * HALF],
                               banks[(NH * (KT + 1) + h) % BANKS_D][0:B, :]).then_inc(rc_hi, 1)

            act.wait_ge(rc_lo, 3 * NH)

            def put(i, n, first):
                per = 2 * QT * NH
                act.wait_ge(out_summed, i * per + n + 1)
                if not first or n >= 4:
                    act.wait_ge(stored[n % 4], (i * (per // 4) + n // 4) * DMA)
                nc.scalar.copy(rows[:, n % 4, :], banks[(n + 2) % 4][:, :]).then_inc(out_copied, 1)
                act.wait_ge(out_copied, i * per + n + 1)
                t, h = n // NH, n % NH
                act.dma_start(out[bass.ds(i * (2 * T) + t * P, P), h * HALF:(h + 1) * HALF], rows[:, n % 4, :]
                              ).then_inc(stored[n % 4], DMA)

            for n in range(2 * QT * NH):
                put(0, n, True)
            with act.Fori(1, B // 2) as i:
                for n in range(2 * QT * NH):
                    put(i, n, False)
            for s in range(4):
                act.wait_ge(stored[s], B * QT * NH // 4 * DMA)

        @block.vector
        def _(dve):
            def low_w(k):
                for which, landed in ((0, w0_landed), (1, w1_landed)):
                    dve.wait_ge(landed[k % STAGE_SLOTS], slot_uses(k) * DMA)
                    if k == 0 and which == 0:
                        dve.wait_ge(ident_made, 2)
                    block_k = stage_w(k, which)[:, k * P:(k + 1) * P]
                    nc.vector.tensor_tensor(block_k, block_k, ident[:, :], ALU.add).then_inc(diag_added, 1)
                dve.wait_ge(hi_made, 2 * k + 1)
                nc.vector.tensor_tensor(w0_lo[:, :, k * P:(k + 1) * P],
                                        stage_w(k, 0).rearrange("p (m c) -> p m c", m=KT),
                                        w0_hi[:, :, k * P:(k + 1) * P], ALU.subtract).then_inc(lo_made, 1)
                dve.wait_ge(hi_made, 2 * k + 2)
                nc.vector.tensor_tensor(w1_lo[:, k, :], stage_w(k, 1), w1_hi[:, k, :], ALU.subtract
                                        ).then_inc(lo_made, 1)

            def low_lora():
                for n, (raw, to) in enumerate(((a1_raw, a1), (b0t_raw, b0w))):
                    dve.wait_ge(lora_hi, n + 1)
                    nc.vector.tensor_tensor(to[:, :, BR:2 * BR].rearrange("p k (b r) -> p b k r", b=B),
                                            raw.rearrange("p (b k r) -> p b k r", b=B, k=KT),
                                            to[:, :, 0:BR].rearrange("p k (b r) -> p b k r", b=B),
                                            ALU.subtract).then_inc(lora_lo, 1)
                dve.wait_ge(lora_hi, 3)
                nc.vector.tensor_tensor(b0w[:, :, 2 * BR + 1], b0_raw[:, :], b0w[:, :, 2 * BR],
                                        ALU.subtract).then_inc(lora_lo, 1)

            def g_add(m, j):
                dve.wait_ge(aux_copied, j + 1)
                nc.vector.tensor_tensor(g_all[:, m, :], banks[6 + j % 2][:, BR:2 * BR], scratch[:, 0:BR],
                                        ALU.add).then_inc(aux_done, 1)

            def low_d(m):
                for h in range(NH):
                    dve.wait_ge(d_hi, NH * m + h + 1)
                    cols = slice(h * HALF, (h + 1) * HALF)
                    nc.vector.tensor_tensor(w0_lo[:, m, cols], banks[(NH * m + h) % BANKS_D][:, :],
                                            w0_hi[:, m, cols], ALU.subtract).then_inc(d_lo, 1)

            def bias_add(k):
                for n, part in enumerate((w1_hi, w1_lo)):
                    if 2 * k + n == 0:
                        dve.wait_ge(bias1_landed, DMA)
                    else:
                        dve.wait_ge(bias_step, 2 * k + n)
                    nc.vector.scalar_tensor_tensor(out=bias_sum, in0=part[:, k, :], scalar=b0_raw[:, k:k + 1],
                                                   in1=bias_sum, op0=ALU.mult, op1=ALU.add).then_inc(bias_step, 1)


            def split_x(i, s, first=False):
                b = i * 2 + s
                dve.wait_ge(x_landed[s], (i + 1) * DMA)
                if not first:
                    dve.wait_ge(out_summed, (b - 1) * (QT * NH))
                raw = stage[:, s, :].rearrange("p (k t) -> p k t", k=KT)
                nc.vector.tensor_copy(x_hi[s], raw).then_inc(x_hi_made, 1)
                dve.wait_ge(x_hi_made, b + 1)
                nc.vector.tensor_tensor(x_lo[s], raw, x_hi[s], ALU.subtract).then_inc(x_ready, 1)

            def factors(i, s, first=False):
                b = i * 2 + s
                to = aa[:, s, 0:KT * 4 * RK].rearrange("p (k c) -> p k c", k=KT)
                g = g_all[:, :, bass.ds(b * RK, RK)]
                a0 = a0_raw[:, s, :].rearrange("p (k r) -> p k r", k=KT)
                dve.wait_ge(a0_landed[s], (i + 1) * DMA)
                if not first:
                    dve.wait_ge(h_summed, b - 1)
                nc.vector.tensor_copy(to[:, :, 0:RK], a0).then_inc(aa_hi, 1)
                nc.vector.tensor_copy(to[:, :, RK:2 * RK], g).then_inc(aa_hi, 1)
                dve.wait_ge(aa_hi, b * 2 + 2)
                nc.vector.tensor_tensor(to[:, :, 3 * RK:4 * RK], g, to[:, :, RK:2 * RK], ALU.subtract)
                nc.vector.tensor_tensor(to[:, :, 2 * RK:3 * RK], a0, to[:, :, 0:RK], ALU.subtract).then_inc(aa_ready, 1)

            def stack_h(i, s):
                b = i * 2 + s
                bank = banks[6 + s]
                dve.wait_ge(h_summed, b + 1)
                nc.vector.tensor_copy(h_tmp, bank[2 * RK:4 * RK, 0:T]).then_inc(h_moved, 1)
                dve.wait_ge(h_moved, b + 1)
                nc.vector.tensor_tensor(h_sum[:, :], bank[0:2 * RK, 0:T], h_tmp, ALU.add).then_inc(h_added, 1)
                dve.wait_ge(h_added, b + 1)
                nc.vector.tensor_copy(h_stack[s][0:2 * RK, :], h_sum[:, :]).then_inc(h_hi, 1)
                nc.vector.tensor_copy(h_stack[s][2 * RK:4 * RK, :], h_sum[:, :]).then_inc(h_hi, 1)
                dve.wait_ge(h_hi, b * 2 + 2)
                nc.vector.tensor_tensor(h_stack[s][4 * RK:6 * RK, :], h_sum[:, :], h_stack[s][0:2 * RK, :],
                                        ALU.subtract).then_inc(h_ready, 1)

            nc.vector.memset(bias_sum, 0.0).then_inc(bias_zeroed, 1)
            for s in range(2):
                nc.vector.memset(aa[:, s, KT * 4 * RK:AA_W].bitcast(F32), 0.0).then_inc(pad_set, 1)
            for k in range(KT):
                low_w(k)
                if k == LORA_AFTER:
                    low_lora()
            for m in range(FIRST_M):
                g_add(m, m)
                low_d(m)
            dve.wait_ge(aux_copied, AUX_ST + 1)
            dve.wait_ge(masks_made, 3)
            nc.vector.tensor_tensor(s_t[:, :], scratch[:, 0:BR], scratch[:, BR:2 * BR], ALU.add).then_inc(st_step, 1)
            nc.vector.tensor_tensor(t_sum[:, :], scratch[:, 2 * BR:2 * BR + 1], scratch[:, 2 * BR + 1:2 * BR + 2],
                                    ALU.add).then_inc(aux_done, 1)
            dve.wait_ge(st_step, 1)
            nc.vector.tensor_tensor(s_t[:, :], s_t[:, :], same_batch[:, :, :].rearrange("p b r -> p (b r)"),
                                    ALU.mult).then_inc(st_step, 1)
            dve.wait_ge(aux_done, AUX_ST + 1)
            nc.vector.tensor_scalar(t_blk[:, :], same_batch[:, :, 0], t_sum[:, 0:1], None, ALU.mult
                                    ).then_inc(st_step, 1)
            for m in range(FIRST_M, KT):
                g_add(m, m + 1)
                if m < KT - 1:
                    for k in range(2 * (m - FIRST_M), 2 * (m - FIRST_M) + 2):
                        bias_add(k)
                else:
                    split_x(0, 0, True)
                    factors(0, 0, True)
                low_d(m)
            for h in range(NH):
                cols = slice(h * HALF, (h + 1) * HALF)
                dve.wait_ge(rc_hi, h + 1)
                nc.vector.scalar_tensor_tensor(out=r_hl[:, 1, cols], in0=banks[(NH * KT + h) % BANKS_D][:, :],
                                               scalar=2.0, in1=r_hl[:, 0, cols], op0=ALU.mult, op1=ALU.subtract
                                               ).then_inc(rc_lo, 1)
            for h in range(NH):
                cols = slice(h * HALF, (h + 1) * HALF)
                dve.wait_ge(rc_hi, NH + h + 1)
                nc.vector.tensor_tensor(b1_hl[:, 1, cols], b1_raw[:, cols], b1_hl[:, 0, cols], ALU.subtract
                                        ).then_inc(rc_lo, 1)
            for h in range(NH):
                cols = slice(h * HALF, (h + 1) * HALF)
                dve.wait_ge(rc_hi, 2 * NH + h + 1)
                nc.vector.tensor_tensor(c_hl[:, 1, cols], banks[(NH * (KT + 1) + h) % BANKS_D][0:B, :],
                                        c_hl[:, 0, cols], ALU.subtract).then_inc(rc_lo, 1)
            for s in range(2):
                nc.vector.memset(h_stack[s][6 * RK:6 * RK + 2, :].bitcast(F32), 1.0).then_inc(ones_set, 1)

            stack_h(0, 0)
            split_x(0, 1, True)
            factors(0, 1, True)
            stack_h(0, 1)
            with dve.Fori(1, B // 2) as i:
                for s in range(2):
                    split_x(i, s)
                    factors(i, s)
                    stack_h(i, s)

        @block.tensor
        def _(pe):
            mm = nc.tensor.matmul

            def d_pass(m, h, k, left, right, start, stop):
                return mm(banks[(NH * m + h) % BANKS_D][:, :], left[:, m, k * P:(k + 1) * P],
                          right[:, k, h * HALF:(h + 1) * HALF], start=start, stop=stop)

            def aux(j, m):
                if j >= 2:
                    pe.wait_ge(aux_done, j - 1)
                for k in range(KT):
                    for n, left in enumerate((w0_hi, w0_lo)):
                        last = mm(banks[6 + j % 2][:, 0:2 * BR], left[:, m, k * P:(k + 1) * P], a1[:, k, :],
                                  start=(k == 0 and n == 0), stop=(k == KT - 1 and n == 1))
                last.then_inc(aux_summed, 1)

            for k in range(KT):
                pe.wait_ge(hi_made, 2 * k + 2)
                for m in range(FIRST_M):
                    for h in range(NH):
                        d_pass(m, h, k, w0_hi, w1_hi, k == 0, False)
                pe.wait_ge(lo_made, 2 * k + 2)
                for m in range(FIRST_M):
                    for h in range(NH):
                        d_pass(m, h, k, w0_hi, w1_lo, False, False)
                        d_pass(m, h, k, w0_lo, w1_hi, False, k == KT - 1)
            pe.wait_ge(lora_lo, 3)
            for m in range(FIRST_M):
                aux(m, m)
            pe.wait_ge(aux_done, AUX_ST - 1)
            for k in range(KT):
                for n in range(2):
                    last = mm(banks[6 + AUX_ST % 2][:, 0:2 * BR + 2], a1[:, k, n * BR:(n + 1) * BR], b0w[:, k, :],
                              start=(k == 0 and n == 0), stop=(k == KT - 1 and n == 1))
            last.then_inc(aux_summed, 1)
            for m in range(FIRST_M, KT):
                aux(m + 1, m)
                for h in range(NH):
                    pe.wait_ge(d_lo, NH * m + h + 1 - BANKS_D)
                    for k in range(KT):
                        d_pass(m, h, k, w0_hi, w1_hi, k == 0, False)
                        d_pass(m, h, k, w0_hi, w1_lo, False, False)
                        last = d_pass(m, h, k, w0_lo, w1_hi, False, k == KT - 1)
                    last.then_inc(d_summed, 1)
            pe.wait_ge(st_step, 3)
            pe.wait_ge(b1_landed, B * DMA)
            for h in range(NH):
                cols = slice(h * HALF, (h + 1) * HALF)
                bank = banks[(NH * KT + h) % BANKS_D]
                pe.wait_ge(d_lo, NH * KT + h + 1 - BANKS_D)
                mm(bank[:, :], s_t[:, :], b1_raw[:, cols], start=True, stop=False)
                for k in range(KT):
                    hi, lo = b0w[:, k, 0:BR], b0w[:, k, BR:2 * BR]
                    mm(bank[:, :], hi, w1_hi[:, k, cols], start=False, stop=False)
                    mm(bank[:, :], hi, w1_lo[:, k, cols], start=False, stop=False)
                    last = mm(bank[:, :], lo, w1_hi[:, k, cols], start=False, stop=(k == KT - 1))
                last.then_inc(r_summed, 1)
            pe.wait_ge(bias_step, 2 * KT)
            for h in range(NH):
                cols = slice(h * HALF, (h + 1) * HALF)
                bank = banks[(NH * (KT + 1) + h) % BANKS_D]
                pe.wait_ge(d_lo, NH * (KT + 1) + h + 1 - BANKS_D)
                mm(bank[0:B, :], ones_b[:, :], bias_sum[:, cols], start=True, stop=False)
                mm(bank[0:B, :], t_blk[:, :], b1_raw[:, cols], start=False, stop=True).then_inc(c_summed, 1)

            def batch(i, s, first):
                b = i * 2 + s
                pe.wait_ge(x_ready, b + 1)
                pe.wait_ge(aa_ready, b + 1)
                if not first:
                    pe.wait_ge(h_added, b - 1)
                for k in range(KT):
                    for n, part in enumerate((x_hi[s], x_lo[s])):
                        last = mm(banks[6 + s][:, 0:T], aa[:, s, k * 4 * RK:k * 4 * RK + P], part[:, k, :],
                                  start=(k == 0 and n == 0), stop=(k == KT - 1 and n == 1))
                last.then_inc(h_summed, 1)
                defer = first and s == 0

                def rank_product(n):
                    q, h = n // NH % QT, n % NH
                    if n % (QT * NH) == 0:
                        pe.wait_ge(h_ready, b + 1)
                    mm(banks[(n + 2) % 4][:, :], h_stack[s][0:STACK, q * P:(q + 1) * P],
                       w1[0:STACK, bass.ds(b * D + h * HALF, HALF)], start=False, stop=True).then_inc(out_summed, 1)

                for n in range(s * QT * NH, (s + 1) * QT * NH):
                    q, h = n // NH % QT, n % NH
                    tok, cols = slice(q * P, (q + 1) * P), slice(h * HALF, (h + 1) * HALF)
                    bank = banks[(n + 2) % 4][:, :]
                    if not (first and n < 4):
                        pe.wait_ge(out_copied, i * (2 * QT * NH) + (n - 3))
                    if first and n == 2:
                        pe.wait_ge(rc_lo, 3 * NH)
                    for k in range(KT):
                        mm(bank, x_hi[s][:, k, tok], w0_hi[:, k, cols], start=(k == 0), stop=False)
                        mm(bank, x_hi[s][:, k, tok], w0_lo[:, k, cols], start=False, stop=False)
                        mm(bank, x_lo[s][:, k, tok], w0_hi[:, k, cols], start=False, stop=False)
                    if not defer:
                        rank_product(n)
                if defer:
                    pe.wait_ge(rb_landed, RB_DMAS * DMA)
                    pe.wait_ge(ones_set, 2)
                    for n in range(QT * NH):
                        rank_product(n)

            pe.wait_ge(d_lo, NH * KT)
            pe.wait_ge(pad_set, 2)
            for s in range(2):
                batch(0, s, True)
            with pe.Fori(1, B // 2) as i:
                for s in range(2):
                    batch(i, s, False)


def kernel(x, itok_B_0_23, itok_B_6_15, L0_cond_W, L0_cond_b, L0_cond_lora_As, L0_cond_lora_Bs,
           L1_cond_base_weight, L1_cond_base_bias, L1_cond_lora_A_w, L1_cond_lora_B_w):
    import numpy as np
    import concourse.bacc as bacc
    from concourse.bass_utils import run_bass_kernel_spmd

    x = np.asarray(x)
    B, T, D = x.shape
    kt = D // P

    def by_partition(a, axis):
        a = np.asarray(a)
        a = np.moveaxis(a, axis, 1)
        a = a.reshape(a.shape[0], kt, P, *a.shape[2:])
        return np.moveaxis(a, 2, 1)

    ins = {
        "xT": by_partition(x, 2),
        "W0": np.asarray(L0_cond_W),
        "W1T": np.asarray(L1_cond_base_weight).T,
        "A0": by_partition(L0_cond_lora_As, 1),
        "B0T": by_partition(L0_cond_lora_Bs, 2),
        "A1T": by_partition(L1_cond_lora_A_w, 2),
        "B1": np.asarray(L1_cond_lora_B_w).transpose(0, 2, 1),
        "b0": np.asarray(L0_cond_b).reshape(kt, P).T,
        "b1": np.asarray(L1_cond_base_bias).reshape(1, D),
        "idx0": np.asarray(itok_B_0_23).reshape(1, B),
        "idx1": np.asarray(itok_B_6_15).reshape(1, B),
    }
    nc = bacc.Bacc("TRN2", target_bir_lowering=False, num_devices=1)
    arrays, args = {}, []
    for name, a in ins.items():
        a = np.ascontiguousarray(a)
        arrays[name] = a
        args.append(nc.dram_tensor(name, a.shape, mybir.dt.from_np(a.dtype), kind="ExternalInput").ap())
    out = nc.dram_tensor("out", (B * T, D), F32, kind="ExternalOutput").ap()
    lora_pair(nc, *args, out)
    r = run_bass_kernel_spmd(nc, [arrays], core_ids=[0])
    return r.results[0]["out"].reshape(B, T, D)
```
